# Optimizing a Trainium2 kernel written in Bass

```python
import numpy as np
import jax
import jax.numpy as jnp

def _softmax(x, axis=-1):
    return jax.nn.softmax(x, axis=axis)

def _gelu(x):
    return jax.nn.gelu(x, approximate=True)

def _silu(x):
    return jax.nn.silu(x)

def _sigmoid(x):
    return jax.nn.sigmoid(x)

def _layernorm(x, axis=-1, eps=1e-05):
    m = jnp.mean(x, axis=axis, keepdims=True)
    v = jnp.var(x, axis=axis, keepdims=True)
    return (x - m) / jnp.sqrt(v + eps)

def _scatter_add(tgt, idx, src, axis=0):
    return tgt.at[idx].add(src)

def _segment_sum(src, seg, n):
    return jax.ops.segment_sum(src, seg, n)
kernel_name = 'mk_cond_resid_d2_seqx_r4_eee6aa'

def setup_inputs(seed: int=0):
    np.random.seed(seed)
    _w = jnp.asarray

    def _rec_inputs():
        import jax
        import jax.numpy as jnp
        _rk = jax.random.key(seed)
        x = 7.22e-05 + 1 * jax.random.normal(jax.random.fold_in(_rk, 1), (8, 512, 256), jnp.float32)
        _lenS = 512 - jax.random.randint(jax.random.fold_in(_rk, 7), (8,), 0, max(1, 512 // 4) + 1, jnp.int32)
        _lenS2 = 512 - jax.random.randint(jax.random.fold_in(_rk, 8), (8,), 0, max(1, 512 // 4) + 1, jnp.int32)
        cond_8 = -0.104238 + 1.01173 * jax.random.normal(jax.random.fold_in(_rk, 11), (8, 8), jnp.float32)
        return (x, cond_8)
    x, cond_8 = _rec_inputs()

    def _L0_cond_setup():
        import jax, jax.numpy as jnp
        import numpy as np
        TOP_K = 2
        NUM_MOE_LAYERS = 12

        def _gemma_mlp(x, gate_w, up_w, down_w):
            g = jnp.einsum('bsh,hi->bsi', x, gate_w)
            u = jnp.einsum('bsh,hi->bsi', x, up_w)
            return jnp.einsum('bsi,ih->bsh', jax.nn.gelu(g, approximate=True) * u, down_w)
        key = jax.random.key(seed)
        ks = jax.random.split(key, 8)
        B, S, H, I, E = (32, 64, 256, 1024, 8)
        std = 0.02
        return {'x': jax.random.normal(ks[0], (B, S, H), jnp.float32), 'router_logits': jax.random.normal(ks[1], (B, E), jnp.float32), 'skill_gate': jax.random.normal(ks[2], (E, H, I), jnp.float32) * std, 'skill_up': jax.random.normal(ks[3], (E, H, I), jnp.float32) * std, 'skill_down': jax.random.normal(ks[4], (E, I, H), jnp.float32) * std, 'shared_gate': jax.random.normal(ks[5], (H, I), jnp.float32) * std, 'shared_up': jax.random.normal(ks[6], (H, I), jnp.float32) * std, 'shared_down': jax.random.normal(ks[7], (I, H), jnp.float32) * std}
    _L0_cond_all = _L0_cond_setup()
    _L0_cond_in = {k: v for k, v in _L0_cond_all.items() if k in ('skill_gate', 'skill_up', 'skill_down', 'shared_gate', 'shared_up', 'shared_down')}
    del _L0_cond_all

    def _L1_cond_setup():
        import jax, jax.numpy as jnp
        import numpy as np
        R = 16
        ALPHA = 32.0
        SCALING = ALPHA / R
        key = jax.random.key(seed)
        ks = jax.random.split(key, 6)
        B, T, C, O, E = (16, 375, 256, 256, 8)
        x = jax.random.normal(ks[0], (B, T, C), dtype=jnp.float32)
        w = jax.random.uniform(ks[1], (B, E), dtype=jnp.float32)
        W_base = jax.random.normal(ks[2], (O, C), dtype=jnp.float32) * 0.02
        b_base = jax.random.normal(ks[3], (O,), dtype=jnp.float32) * 0.02
        As = jax.random.normal(ks[4], (E, R, C), dtype=jnp.float32) * 0.02
        Bs = jax.random.normal(ks[5], (E, O, R), dtype=jnp.float32) * 0.02
        return {'x': x, 'w': w, 'W_base': W_base, 'b_base': b_base, 'As': As, 'Bs': Bs}
    _L1_cond_all = _L1_cond_setup()
    _L1_cond_in = {k: v for k, v in _L1_cond_all.items() if k in ('W_base', 'b_base', 'As', 'Bs')}
    del _L1_cond_all
    return {'x': x, 'cond_8': cond_8, 'L0_cond_skill_gate': _L0_cond_in['skill_gate'], 'L0_cond_skill_up': _L0_cond_in['skill_up'], 'L0_cond_skill_down': _L0_cond_in['skill_down'], 'L0_cond_shared_gate': _L0_cond_in['shared_gate'], 'L0_cond_shared_up': _L0_cond_in['shared_up'], 'L0_cond_shared_down': _L0_cond_in['shared_down'], 'L1_cond_W_base': _L1_cond_in['W_base'], 'L1_cond_b_base': _L1_cond_in['b_base'], 'L1_cond_As': _L1_cond_in['As'], 'L1_cond_Bs': _L1_cond_in['Bs']}

def reference(x, cond_8, L0_cond_skill_gate, L0_cond_skill_up, L0_cond_skill_down, L0_cond_shared_gate, L0_cond_shared_up, L0_cond_shared_down, L1_cond_W_base, L1_cond_b_base, L1_cond_As, L1_cond_Bs):
    import jax
    import jax.numpy as jnp

    def _L0_cond_ref(x, router_logits, skill_gate, skill_up, skill_down, shared_gate, shared_up, shared_down):
        import jax, jax.numpy as jnp
        import numpy as np
        TOP_K = 2
        NUM_MOE_LAYERS = 12

        def _gemma_mlp(x, gate_w, up_w, down_w):
            g = jnp.einsum('bsh,hi->bsi', x, gate_w)
            u = jnp.einsum('bsh,hi->bsi', x, up_w)
            return jnp.einsum('bsi,ih->bsh', jax.nn.gelu(g, approximate=True) * u, down_w)
        B = x.shape[0]
        E = skill_gate.shape[0]
        rw = jax.nn.softmax(router_logits.astype(jnp.float32), axis=-1)
        w, sel = jax.lax.top_k(rw, TOP_K)
        w = w / w.sum(axis=-1, keepdims=True)
        w = w.astype(x.dtype)
        scale = 1.0 / NUM_MOE_LAYERS
        w = scale * w + (1.0 - scale) * jax.lax.stop_gradient(w)
        dense_w = jnp.zeros((B, E), x.dtype).at[jnp.arange(B)[:, None], sel].add(w)

        def step(acc, params):
            g, u, d, we = params
            return (acc + we[:, None, None] * _gemma_mlp(x, g, u, d), None)
        out, _ = jax.lax.scan(step, jnp.zeros_like(x), (skill_gate, skill_up, skill_down, dense_w.T))
        out = out + _gemma_mlp(x, shared_gate, shared_up, shared_down)
        return out

    def _L1_cond_ref(x, w, W_base, b_base, As, Bs):
        import jax, jax.numpy as jnp
        import numpy as np
        R = 16
        ALPHA = 32.0
        SCALING = ALPHA / R
        out = jnp.einsum('btc,oc->bto', x, W_base) + b_base
        h = jnp.einsum('btc,erc->bter', x, As)
        lora = jnp.einsum('bter,eor,be->bto', h, Bs, w)
        return out + lora * SCALING
    x = x + _L0_cond_ref(x, cond_8, L0_cond_skill_gate, L0_cond_skill_up, L0_cond_skill_down, L0_cond_shared_gate, L0_cond_shared_up, L0_cond_shared_down)
    x = x + _L1_cond_ref(x, cond_8, L1_cond_W_base, L1_cond_b_base, L1_cond_As, L1_cond_Bs)
    return x

_drawn_inputs = setup_inputs


def setup_inputs(seed=0):
    import zlib

    import numpy as np

    out = dict(_drawn_inputs(seed))
    spreads = {}
    factors = {'L1_cond_b_base': 3.275}
    for name, (base, spread) in spreads.items():
        noise = np.random.default_rng([zlib.crc32(name.encode()), seed]).standard_normal(out[name].shape)
        drawn = base * np.exp(spread * noise) if base else spread * noise
        out[name] = jnp.asarray(drawn.astype(out[name].dtype))
    for name, factor in factors.items():
        out[name] = (out[name] * factor).astype(out[name].dtype)
    return out
```

```python
from contextlib import ExitStack

import concourse.bass as bass
from concourse import mybir

ALU = mybir.AluOpType
ACT = mybir.ActivationFunctionType
AX_X = mybir.AxisListType.X
F32 = mybir.dt.float32
F32R = mybir.dt.float32r
U32 = mybir.dt.uint32

P = 128
TOP_K = 2
MOE_SCALE = 1.0 / 12
LORA_SCALE = 32.0 / 16


def cond_resid_kernel(nc, x, cond, skill_gate, skill_up, skill_down, shared_gate, shared_up,
                      shared_down, w_base, b_base, lora_a, lora_b, out):
    B, S, H = x.shape
    E, _, I = skill_gate.shape
    R = lora_a.shape[1]
    HC = H // P
    IC = I // P
    PAIRS = IC // 2
    PW = 2 * P
    TT = S // P
    SLOTS = 1 + TOP_K
    K = SLOTS * IC
    assert HC == 2 and TT == 4 and E * R == P and H == 256 and S == 512 and E == 8

    L1_STEP = 3
    FOLD_STEP = 9
    TURN_STEP = 13

    def split_at(k):
        if k % 2 == 0 and 2 <= k < 2 + 2 * PAIRS:
            return 0, (k - 2) // 2
        if k % 2 == 0 and IC + 4 <= k < IC + 4 + 2 * PAIRS:
            return 1, (k - IC - 4) // 2
        return None

    with ExitStack() as ctx:
        def sb(name, shape, dt=F32):
            return ctx.enter_context(nc.sbuf_tensor(name, shape, dt))

        def psum(name):
            return ctx.enter_context(nc.psum_tensor(name, [P, 512], F32))

        def sem(name):
            return ctx.enter_context(nc.semaphore(name))

        raw_gu = sb("raw_gu", [P, PAIRS, 2 * HC, PW])
        raw_dn = sb("raw_dn", [P, PAIRS, 2, H])
        sh_gu = [sb(f"sh_gu_{n}", [P, PAIRS, 2 * HC, PW], F32R) for n in ("hi", "lo")]
        sh_dn = [sb(f"sh_dn_{n}", [P, PAIRS, 2, H], F32R) for n in ("hi", "lo")]
        ex_gu = [sb(f"ex_gu_{n}", [P, PAIRS, 2 * HC, PW], F32R) for n in ("hi", "lo")]
        ex_dn = [sb(f"ex_dn_{n}", [P, PAIRS, 2, H], F32R) for n in ("hi", "lo")]
        x_nat = sb("x_nat", [P, TT, H])
        x_next = [sb(f"x_next_{n}", [P, HC * S], F32R) for n in ("hi", "lo")]
        x_cur = [sb(f"x_cur_{n}", [P, HC * S], F32R) for n in ("hi", "lo")]
        x_full = sb("x_full", [P, HC * S])
        gelu = sb("gelu", [P, 2, S])
        inner = sb("inner", [P, 2, S])
        inner_s = [sb(f"inner_{n}", [P, 3, S], F32R) for n in ("hi", "lo")]
        x1 = sb("x1", [P, HC * S])
        x1_s = [sb(f"x1_{n}", [P, HC, S], F32R) for n in ("hi", "lo")]
        a_nat = sb("a_nat", [P, H])
        a_s = [sb(f"a_{n}", [P, H], F32R) for n in ("hi", "lo")]
        b_nat = sb("b_nat", [P, HC, E * R])
        b_t = sb("b_t", [P, H])
        bw = sb("bw", [P, H])
        bw_s = [sb(f"bw_{n}", [P, H], F32R) for n in ("hi", "lo")]
        w_nat = sb("w_nat", [P, HC, H])
        w_id = sb("w_id", [P, HC * H])
        w_eff = sb("w_eff", [P, HC * H])
        w_eff_s = [sb(f"w_eff_{n}", [P, HC, H], F32R) for n in ("hi", "lo")]
        bias = sb("bias", [P, 2, H])
        o_row = sb("o_row", [P, TT, H])
        logits = sb("logits", [P, B, E])
        top = sb("top", [P, B, 8])
        top_e = sb("top_e", [P, B, 8], U32)
        shifted = sb("shifted", [P, B, 8])
        expd = sb("expd", [P, B, 8])
        total = sb("total", [P, B])
        rtotal = sb("rtotal", [P, B])
        prob = sb("prob", [P, B, TOP_K])
        psumk = sb("psumk", [P, B])
        rpsumk = sb("rpsumk", [P, B])
        wk = sb("wk", [P, B, TOP_K])
        wk_rest = sb("wk_rest", [P, B, TOP_K])
        lora_w = sb("lora_w", [P, B])
        coef = sb("coef", [P, B, 3])
        coef_now = sb("coef_now", [P, 3])
        ident = sb("ident", [P, P])

        ps_gate = [psum(f"ps_gate{i}") for i in range(2)]
        ps_up = [psum(f"ps_up{i}") for i in range(2)]
        ps_acc = [psum(f"ps_acc{i}") for i in range(HC)]
        ps_misc = [psum(f"ps_misc{i}") for i in range(2)]

        raw_landed = [sem(f"raw_landed{j}") for j in range(PAIRS)]
        x_landed = sem("x_landed")
        cond_landed = sem("cond_landed")
        lora_w_landed = sem("lora_w_landed")
        layer1_landed = sem("layer1_landed")
        out_landed = sem("out_landed")
        gate_done = sem("gate_done")
        up_done = sem("up_done")
        down_done = sem("down_done")
        sum_done = sem("sum_done")
        turned = sem("turned")
        turned_w = sem("turned_w")
        fold_done = sem("fold_done")
        l1_done = sem("l1_done")
        exp_done = sem("exp_done")
        gelu_done = sem("gelu_done")
        inner_hi = sem("inner_hi")
        weights_hi = sem("weights_hi")
        shared_hi = sem("shared_hi")
        x_hi = sem("x_hi")
        x_lo_in = sem("x_lo_in")
        x1_hi = sem("x1_hi")
        a_hi = sem("a_hi")
        bw_hi = sem("bw_hi")
        w_eff_hi = sem("w_eff_hi")
        routed = sem("routed")
        experts_known = sem("experts_known")
        coef_done = sem("coef_done")
        coef_ready = sem("coef_ready")
        mul_done = sem("mul_done")
        inner_ready = sem("inner_ready")
        weights_ready = sem("weights_ready")
        shared_ready = sem("shared_ready")
        x_split = sem("x_split")
        x_hi_in = sem("x_hi_in")
        x_full_done = sem("x_full_done")
        x1_done = sem("x1_done")
        x1_ready = sem("x1_ready")
        a_ready = sem("a_ready")
        w_turned = sem("w_turned")
        w_id_done = sem("w_id_done")
        b_t_done = sem("b_t_done")
        bw_done = sem("bw_done")
        bw_ready = sem("bw_ready")
        w_eff_done = sem("w_eff_done")
        w_eff_ready = sem("w_eff_ready")
        o_ready = sem("o_ready")
        ident_zero = sem("ident_zero")
        ident_ready = sem("ident_ready")

        x_rows = x.rearrange("b (p t) h -> b p t h", t=TT)
        out_rows = out.rearrange("b (p t) h -> b p t h", t=TT)
        sk_gate = skill_gate.rearrange("e (c p) i -> e p c i", p=P)
        sk_up = skill_up.rearrange("e (c p) i -> e p c i", p=P)
        sk_down = skill_down.rearrange("e (j c p) h -> e j p c h", p=P, c=2)

        block = ctx.enter_context(nc.Block())

        @block.sync
        def _(sp):
            def load_pair(j, gate, up, down):
                cols = slice(j * PW, (j + 1) * PW)
                sp.dma_start(raw_gu[:, j, 0:HC, :], gate[:, :, cols]).then_inc(raw_landed[j], 16)
                sp.dma_start(raw_gu[:, j, HC:2 * HC, :], up[:, :, cols]).then_inc(raw_landed[j], 16)
                sp.dma_start(raw_dn[:, j, :, :], down[j]).then_inc(raw_landed[j], 16)

            def load_routed(b, s, pairs):
                e = sp.value_load(top_e[0:1, b, s:s + 1], min_val=0, max_val=E - 1)
                gate = sk_gate[bass.ds(e, 1)].rearrange("e p c i -> (e p) c i")
                up = sk_up[bass.ds(e, 1)].rearrange("e p c i -> (e p) c i")
                down = sk_down[bass.ds(e, 1)].rearrange("e j p c h -> (e j) p c h")
                for j in pairs:
                    sp.wait_ge(weights_ready, b * (TOP_K * PAIRS) + s * PAIRS + j + 1)
                    load_pair(j, gate, up, down)

            def batch_row(b, first, last):
                if not last:
                    sp.wait_ge(turned, b * 2 + 2)
                    sp.dma_start(x_nat[:], x_rows[b + 1]).then_inc(x_landed, 16)
                load_routed(b, 1, range(0, 2))
                if not first:
                    store_row(b - 1)
                load_routed(b, 1, range(2, PAIRS))
                if not last:
                    load_routed(b + 1, 0, range(PAIRS))

            def store_row(b):
                for i in range(2):
                    sp.wait_ge(o_ready, b * 2 + i + 1)
                    tiles = slice(2 * i, 2 * i + 2)
                    sp.dma_start(out_rows[b][:, tiles], o_row[:, tiles]).then_inc(out_landed, 16)

            sg = shared_gate.rearrange("(c p) i -> p c i", p=P)
            su = shared_up.rearrange("(c p) i -> p c i", p=P)
            sd = shared_down.rearrange("(j c p) h -> j p c h", p=P, c=2)
            sp.dma_start(x_nat[:], x_rows[0]).then_inc(x_landed, 16)
            for j in range(PAIRS):
                load_pair(j, sg, su, sd)
            sp.wait_ge(experts_known, 1)
            load_routed(0, 0, range(PAIRS))
            batch_row(0, True, False)
            with sp.Fori(1, B - 1) as b:
                batch_row(b, False, False)
            batch_row(B - 1, False, True)
            store_row(B - 1)
            sp.wait_ge(out_landed, 32 * B)

        @block.gpsimd
        def _(pool):
            nc.gpsimd.memset(ident[:], 0.0).then_inc(ident_zero, 1)
            pool.wait_ge(ident_zero, 1)
            nc.gpsimd.affine_select(out=ident[:], in_=ident[:], compare_op=ALU.not_equal, fill=1.0,
                                    base=0, pattern=[[-1, P]], channel_multiplier=1)\
                .then_inc(ident_ready, 1)
            pool.dma_start(a_nat[:], lora_a.rearrange("e r c -> (e r) c")).then_inc(layer1_landed, 16)
            for c in range(HC):
                pool.dma_start(b_nat[:, c, :].rearrange("p (e r) -> p e r", e=E),
                               lora_b[:, c * P:(c + 1) * P, :].rearrange("e p r -> p e r"))\
                    .then_inc(layer1_landed, 16)
            pool.dma_start(w_nat[:], w_base.rearrange("(c p) h -> p c h", p=P)).then_inc(layer1_landed, 16)
            for i in range(2):
                pool.dma_start(bias[:, i, :], b_base.partition_broadcast(P)).then_inc(layer1_landed, 16)
            with nc.allow_non_contiguous_dma(reason="64 scalars, each to 16 partitions"):
                for e in range(E):
                    pool.dma_start(lora_w[e * R:(e + 1) * R, :],
                                   cond[:, e].partition_broadcast(R)).then_inc(lora_w_landed, 16)

        @block.tensor
        def _(pe):
            def product(dst, left, right, start, stop):
                passes = [(0, 0), (0, 1), (1, 0)]
                for n, (a, b) in enumerate(passes):
                    last = pe.matmul(dst, left[a], right[b], start=start and n == 0,
                                     stop=stop and n == len(passes) - 1)
                return last

            def weights_of(k):
                gu, dn = (sh_gu, sh_dn) if k < IC else (ex_gu, ex_dn)
                return gu, dn, k % IC // 2

            def project(k, dst, part):
                gu, _, j = weights_of(k)
                cols = slice(k % 2 * P, k % 2 * P + P)
                for c in range(HC):
                    last = product(dst[:], [w[:, j, part * HC + c, cols] for w in gu],
                                   [v[:, c * S:(c + 1) * S] for v in x_cur], c == 0, c == HC - 1)
                return last

            def down(b, k, first):
                _, dn, j = weights_of(k)
                if first and k < IC and k % 2 == 0:
                    pe.wait_ge(weights_ready, k // 2 + 1)
                pe.wait_ge(inner_ready, b * K + k + 1)
                for m in range(HC):
                    last = product(ps_acc[m][:], [w[:, j, k % 2, m * P:(m + 1) * P] for w in dn],
                                   [v[:, k % 3, :] for v in inner_s], k == 0, k == K - 1)
                    if k == K - 1 and m < HC - 1:
                        last.then_inc(sum_done, 1)
                last.then_inc(down_done, 1)

            def turn_x(b):
                pe.wait_ge(x_landed, b * 16 + 16)
                for c in range(HC):
                    for t in range(TT):
                        last = pe.transpose(ps_misc[c][:, t * P:(t + 1) * P],
                                            x_nat[:, t, c * P:(c + 1) * P], ident[:])
                    last.then_inc(turned, 1)

            def fold(b):
                pe.wait_ge(bw_ready, b + 1)
                for c in range(HC):
                    last = product(ps_misc[0][:, c * H:(c + 1) * H],
                                   [v[:, c * P:(c + 1) * P] for v in a_s], [v[:] for v in bw_s],
                                   True, True)
                last.then_inc(fold_done, 1)

            def layer1(b):
                pe.wait_ge(x1_ready, b + 1)
                pe.wait_ge(w_eff_ready, b + 1)
                for t in range(TT):
                    for c in range(HC):
                        last = product(ps_misc[t // 2][:, t % 2 * H:(t % 2 + 1) * H],
                                       [v[:, c, t * P:(t + 1) * P] for v in x1_s],
                                       [w[:, c, :] for w in w_eff_s], c == 0, c == HC - 1)
                    if t % 2 == 1:
                        last.then_inc(l1_done, 1)

            def turn_constants():
                pe.wait_ge(layer1_landed, 6 * 16)
                for c in range(HC):
                    for o in range(HC):
                        pe.transpose(ps_misc[0][:, c * H + o * P:c * H + (o + 1) * P],
                                     w_nat[:, o, c * P:(c + 1) * P], ident[:])
                for o in range(HC):
                    last = pe.transpose(ps_misc[1][:, o * P:(o + 1) * P], b_nat[:, o, :], ident[:])
                last.then_inc(turned_w, 1)

            def batch_row(b, first, last):
                if first:
                    pe.wait_ge(x_split, 1)
                else:
                    pe.wait_ge(x_hi_in, b)
                    pe.wait_ge(x_lo_in, b)
                for k in range(K):
                    if k % 2 == 0 and k >= IC:
                        pe.wait_ge(weights_ready, b * (TOP_K * PAIRS) + PAIRS + (k - IC) // 2 + 1)
                    elif k < IC and first:
                        pe.wait_ge(shared_ready, k + 1)
                    if k >= 2 or not first:
                        pe.wait_ge(gelu_done, b * K + k - 1)
                    project(k, ps_gate[k % 2], 0).then_inc(gate_done, 1)
                    if k >= 2 or not first:
                        pe.wait_ge(mul_done, b * K + k - 1)
                    project(k, ps_up[k % 2], 1).then_inc(up_done, 1)
                    if k == 2 and not first:
                        pe.wait_ge(x1_done, b * 2)
                    if k >= 2:
                        down(b, k - 2, first)
                    if k == L1_STEP and first:
                        turn_constants()
                    if k == L1_STEP and not first:
                        layer1(b - 1)
                    if k == FOLD_STEP:
                        if first:
                            pe.wait_ge(w_turned, 1)
                        else:
                            pe.wait_ge(o_ready, b * 2)
                        fold(b)
                    if k == TURN_STEP and not last:
                        pe.wait_ge(w_eff_done, b + 1)
                        turn_x(b + 1)
                down(b, K - 2, first)
                down(b, K - 1, first)

            pe.wait_ge(ident_ready, 1)
            turn_x(0)
            batch_row(0, True, False)
            with pe.Fori(1, B - 1) as b:
                batch_row(b, False, False)
            batch_row(B - 1, False, True)
            layer1(B - 1)

        @block.scalar
        def _(act):
            def take_hi(dst, src):
                return nc.scalar.copy(dst, src)

            def split_shared(j):
                act.wait_ge(raw_landed[j], 48)
                for i in range(2):
                    cols = slice(i * P, (i + 1) * P)
                    take_hi(sh_gu[0][:, j, :, cols], raw_gu[:, j, :, cols]).then_inc(shared_hi, 1)
                take_hi(sh_dn[0][:, j], raw_dn[:, j]).then_inc(weights_hi, 1)

            def split_routed(b, s, j):
                act.wait_ge(raw_landed[j], b * (48 * TOP_K) + 48 * (s + 2))
                if s > 0:
                    act.wait_ge(down_done, b * K + s * IC + 2 * j + 2)
                take_hi(ex_gu[0][:, j], raw_gu[:, j])
                take_hi(ex_dn[0][:, j], raw_dn[:, j]).then_inc(weights_hi, 1)

            def x_next_hi(b):
                for c in range(HC):
                    act.wait_ge(turned, b * 2 + c + 1)
                    take_hi(x_next[0][:, c * S:(c + 1) * S], ps_misc[c][:]).then_inc(x_hi, 1)

            def layer1_hi(b):
                for c in range(HC):
                    act.wait_ge(x1_done, b * 2 + c + 1)
                    take_hi(x1_s[0][:, c], x1[:, c * S:(c + 1) * S]).then_inc(x1_hi, 1)

            def batch_row(b, first, last):
                if not first:
                    layer1_hi(b - 1)
                for k in range(K):
                    act.wait_ge(gate_done, b * K + k + 1)
                    if k >= 2 or not first:
                        act.wait_ge(mul_done, b * K + k - 1)
                    nc.scalar.activation(gelu[:, k % 2, :], ps_gate[k % 2][:],
                                         ACT.Gelu_apprx_tanh).then_inc(gelu_done, 1)
                    if k == FOLD_STEP - 3:
                        act.wait_ge(bw_done, b + 1)
                        take_hi(bw_s[0][:], bw[:]).then_inc(bw_hi, 1)
                    if k == FOLD_STEP + 2:
                        act.wait_ge(w_eff_done, b + 1)
                        take_hi(w_eff_s[0][:].rearrange("p c h -> p (c h)"), w_eff[:]).then_inc(w_eff_hi, 1)
                    if k == TURN_STEP + 2 and not last:
                        x_next_hi(b + 1)
                    if k == K - 1 and not last:
                        act.wait_ge(up_done, b * K + K)
                        act.wait_ge(x_split, b + 2)
                        nc.scalar.copy(x_cur[1][:], x_next[1][:].bitcast(F32)).then_inc(x_lo_in, 1)
                    act.wait_ge(mul_done, b * K + k + 1)
                    if k >= 3 or not first:
                        act.wait_ge(down_done, b * K + k - 2)
                    take_hi(inner_s[0][:, k % 3, :], inner[:, k % 2, :]).then_inc(inner_hi, 1)
                    if first and k in (0, 2):
                        split_shared(2 + k // 2)
                    if first and k == L1_STEP:
                        act.wait_ge(layer1_landed, 6 * 16)
                        take_hi(a_s[0][:], a_nat[:]).then_inc(a_hi, 1)
                    if split_at(k):
                        split_routed(b, *split_at(k))

            act.dma_start(logits[:], cond.partition_broadcast(P)).then_inc(cond_landed, 16)
            act.wait_ge(routed, 2)
            nc.scalar.activation(expd[:], shifted[:], ACT.Exp).then_inc(exp_done, 1)
            for c in range(HC):
                act.wait_ge(turned, c + 1)
                take_hi(x_cur[0][:, c * S:(c + 1) * S], ps_misc[c][:]).then_inc(x_hi, 1)
            split_shared(0)
            split_shared(1)
            batch_row(0, True, False)
            with act.Fori(1, B - 1) as b:
                batch_row(b, False, False)
            batch_row(B - 1, False, True)
            layer1_hi(B - 1)

        @block.vector
        def _(dve):
            V = nc.vector

            def take_lo(dst, src, hi):
                return V.tensor_tensor(dst, src, hi.bitcast(F32), ALU.subtract)

            def split_shared(j):
                for i in range(2):
                    cols = slice(i * P, (i + 1) * P)
                    dve.wait_ge(shared_hi, 2 * j + i + 1)
                    take_lo(sh_gu[1][:, j, :, cols], raw_gu[:, j, :, cols], sh_gu[0][:, j, :, cols])\
                        .then_inc(shared_ready, 1)
                dve.wait_ge(weights_hi, j + 1)
                take_lo(sh_dn[1][:, j], raw_dn[:, j], sh_dn[0][:, j]).then_inc(weights_ready, 1)

            def split_routed(b, s, j):
                dve.wait_ge(weights_hi, b * (TOP_K * PAIRS) + PAIRS * (s + 1) + j + 1)
                take_lo(ex_gu[1][:, j], raw_gu[:, j], ex_gu[0][:, j])
                take_lo(ex_dn[1][:, j], raw_dn[:, j], ex_dn[0][:, j]).then_inc(weights_ready, 1)

            def route():
                dve.wait_ge(cond_landed, 16)
                for b in range(B):
                    last = V.max(top[:, b], logits[:, b])
                last.then_inc(routed, 1)
                dve.wait_ge(routed, 1)
                V.tensor_tensor(shifted[:], top[:], top[:, :, 0:1].to_broadcast([P, B, 8]), ALU.subtract)\
                    .then_inc(routed, 1)

            def route_weights():
                for b in range(B):
                    last = V.max_index(top_e[:, b], top[:, b], logits[:, b])
                last.then_inc(experts_known, 1)
                dve.wait_ge(exp_done, 1)
                V.tensor_reduce(total[:], expd[:], AX_X, ALU.add).then_inc(routed, 1)
                dve.wait_ge(routed, 3)
                V.reciprocal(rtotal[:], total[:]).then_inc(routed, 1)
                dve.wait_ge(routed, 4)
                V.tensor_tensor(prob[:], expd[:, :, 0:TOP_K],
                                rtotal[:].unsqueeze(2).to_broadcast([P, B, TOP_K]), ALU.mult)\
                    .then_inc(routed, 1)
                dve.wait_ge(routed, 5)
                V.tensor_reduce(psumk[:], prob[:], AX_X, ALU.add).then_inc(routed, 1)
                dve.wait_ge(routed, 6)
                V.reciprocal(rpsumk[:], psumk[:]).then_inc(routed, 1)
                dve.wait_ge(routed, 7)
                V.tensor_tensor(wk[:], prob[:], rpsumk[:].unsqueeze(2).to_broadcast([P, B, TOP_K]),
                                ALU.mult).then_inc(routed, 1)
                dve.wait_ge(routed, 8)
                V.tensor_scalar(wk_rest[:], wk[:], 1.0 - MOE_SCALE, None, ALU.mult).then_inc(routed, 1)
                dve.wait_ge(routed, 9)
                V.scalar_tensor_tensor(out=coef[:, :, 0:TOP_K], in0=wk[:], scalar=MOE_SCALE, in1=wk_rest[:],
                                       op0=ALU.mult, op1=ALU.add).then_inc(coef_done, 1)

            def layer1_constants():
                dve.wait_ge(lora_w_landed, 16 * E)
                V.tensor_scalar(coef[:, :, TOP_K], lora_w[:], LORA_SCALE, None, ALU.mult).then_inc(coef_done, 1)
                dve.wait_ge(a_hi, 1)
                take_lo(a_s[1][:], a_nat[:], a_s[0][:]).then_inc(a_ready, 1)
                dve.wait_ge(turned_w, 1)
                V.tensor_copy(b_t[:], ps_misc[1][:, 0:H]).then_inc(b_t_done, 1)
                V.tensor_copy(w_id[:], ps_misc[0][:]).then_inc(w_turned, 1)
                dve.wait_ge(w_turned, 1)
                for c in range(HC):
                    d = w_id[:, c * H + c * P:c * H + (c + 1) * P]
                    V.tensor_tensor(d, d, ident[:], ALU.add).then_inc(w_id_done, 1)

            def x_next_lo(b):
                for c in range(HC):
                    dve.wait_ge(x_hi, b * 2 + c + 1)
                    last = take_lo(x_next[1][:, c * S:(c + 1) * S], ps_misc[c][:],
                                   x_next[0][:, c * S:(c + 1) * S])
                last.then_inc(x_split, 1)

            def layer1_sum(b):
                dve.wait_ge(x_full_done, b + 1)
                for m in range(HC):
                    if m < HC - 1:
                        dve.wait_ge(sum_done, b + 1)
                    else:
                        dve.wait_ge(down_done, b * K + K)
                    V.tensor_tensor(x1[:, m * S:(m + 1) * S], ps_acc[m][:], x_full[:, m * S:(m + 1) * S],
                                    ALU.add).then_inc(x1_done, 1)

            def layer1_lo(b):
                for c in range(HC):
                    dve.wait_ge(x1_hi, b * 2 + c + 1)
                    last = take_lo(x1_s[1][:, c], x1[:, c * S:(c + 1) * S], x1_s[0][:, c])
                last.then_inc(x1_ready, 1)

            def finish_row(b, first):
                if not first:
                    dve.wait_ge(out_landed, b * 32)
                for i in range(2):
                    dve.wait_ge(l1_done, b * 2 + i + 1)
                    V.tensor_tensor(o_row[:, 2 * i:2 * i + 2, :],
                                    ps_misc[i][:].rearrange("p (t h) -> p t h", t=2), bias[:], ALU.add)\
                        .then_inc(o_ready, 1)

            def batch_row(b, first, last):
                if not first:
                    layer1_sum(b - 1)
                if not first:
                    layer1_lo(b - 1)
                for k in range(K):
                    dve.wait_ge(gelu_done, b * K + k + 1)
                    dve.wait_ge(up_done, b * K + k + 1)
                    if k < IC:
                        V.tensor_tensor(inner[:, k % 2, :], gelu[:, k % 2, :], ps_up[k % 2][:], ALU.mult)\
                            .then_inc(mul_done, 1)
                    else:
                        if k == IC:
                            dve.wait_ge(coef_ready, b + 1)
                        s = k // IC - 1
                        V.scalar_tensor_tensor(out=inner[:, k % 2, :], in0=gelu[:, k % 2, :],
                                               scalar=coef_now[:, s:s + 1], in1=ps_up[k % 2][:],
                                               op0=ALU.mult, op1=ALU.mult).then_inc(mul_done, 1)
                    if k == K - 1 and not last:
                        V.tensor_copy(x_cur[0][:], x_next[0][:].bitcast(F32)).then_inc(x_hi_in, 1)
                    dve.wait_ge(inner_hi, b * K + k + 1)
                    take_lo(inner_s[1][:, k % 3, :], inner[:, k % 2, :], inner_s[0][:, k % 3, :])\
                        .then_inc(inner_ready, 1)
                    if first and k in (0, 2):
                        split_shared(2 + k // 2)
                    if split_at(k):
                        split_routed(b, *split_at(k))
                    if k == 1:
                        if first:
                            dve.wait_ge(x_split, 1)
                        else:
                            dve.wait_ge(x_hi_in, b)
                            dve.wait_ge(x_lo_in, b)
                        V.tensor_tensor(x_full[:], x_cur[0][:].bitcast(F32), x_cur[1][:].bitcast(F32),
                                        ALU.add).then_inc(x_full_done, 1)
                    if k == L1_STEP + 1 and not first:
                        finish_row(b - 1, False)
                    if k == L1_STEP and first:
                        layer1_constants()
                        dve.wait_ge(coef_done, 2)
                    if k == L1_STEP + 1:
                        V.tensor_copy(coef_now[:], coef[:, b, :]).then_inc(coef_ready, 1)
                    if k == FOLD_STEP - 4:
                        dve.wait_ge(coef_ready, b + 1)
                        dve.wait_ge(b_t_done, 1)
                        V.tensor_scalar(bw[:], b_t[:], coef_now[:, TOP_K:TOP_K + 1], None, ALU.mult)\
                            .then_inc(bw_done, 1)
                    if k == FOLD_STEP - 3:
                        dve.wait_ge(bw_hi, b + 1)
                        take_lo(bw_s[1][:], bw[:], bw_s[0][:]).then_inc(bw_ready, 1)
                    if k == FOLD_STEP + 1:
                        dve.wait_ge(fold_done, b + 1)
                        dve.wait_ge(w_id_done, HC)
                        V.tensor_tensor(w_eff[:], ps_misc[0][:], w_id[:], ALU.add).then_inc(w_eff_done, 1)
                    if k == FOLD_STEP + 2:
                        dve.wait_ge(w_eff_hi, b + 1)
                        take_lo(w_eff_s[1][:].rearrange("p c h -> p (c h)"), w_eff[:],
                                w_eff_s[0][:].rearrange("p c h -> p (c h)")).then_inc(w_eff_ready, 1)
                    if k == TURN_STEP + 2 and not last:
                        x_next_lo(b + 1)

            route()
            for c in range(HC):
                dve.wait_ge(x_hi, c + 1)
                last = take_lo(x_cur[1][:, c * S:(c + 1) * S], ps_misc[c][:], x_cur[0][:, c * S:(c + 1) * S])
            last.then_inc(x_split, 1)
            split_shared(0)
            route_weights()
            split_shared(1)
            batch_row(0, True, False)
            with dve.Fori(1, B - 1) as b:
                batch_row(b, False, False)
            batch_row(B - 1, False, True)
            layer1_sum(B - 1)
            layer1_lo(B - 1)
            finish_row(B - 1, False)


_INS = ["x", "cond_8", "L0_cond_skill_gate", "L0_cond_skill_up", "L0_cond_skill_down", "L0_cond_shared_gate",
        "L0_cond_shared_up", "L0_cond_shared_down", "L1_cond_W_base", "L1_cond_b_base", "L1_cond_As",
        "L1_cond_Bs"]


def kernel(**inputs):
    import numpy as _np
    import concourse.bacc as _bacc
    from concourse import mybir as _mybir
    from concourse.bass_utils import run_bass_kernel_spmd as _run

    nc = _bacc.Bacc("TRN2", target_bir_lowering=False, num_devices=1)
    arrays, args = {}, []
    for name in _INS:
        a = _np.ascontiguousarray(inputs[name])
        arrays[f"in_{name}_dram"] = a
        args.append(nc.dram_tensor(f"in_{name}_dram", a.shape, _mybir.dt.from_np(a.dtype), kind="ExternalInput").ap())
    shape = inputs["x"].shape
    args.append(nc.dram_tensor("out_0_dram", shape, _mybir.dt.float32, kind="ExternalOutput").ap())
    cond_resid_kernel(nc, *args)
    r = _run(nc, [arrays], core_ids=[0])
    return r.results[0]["out_0_dram"]
```
